# Optimizing a Trainium2 kernel written in Bass

```python
import numpy as np
import jax
import jax.numpy as jnp

def _softmax(x, axis=-1):
    return jax.nn.softmax(x, axis=axis)

def _gelu(x):
    return jax.nn.gelu(x, approximate=True)

def _silu(x):
    return jax.nn.silu(x)

def _sigmoid(x):
    return jax.nn.sigmoid(x)

def _layernorm(x, axis=-1, eps=1e-05):
    m = jnp.mean(x, axis=axis, keepdims=True)
    v = jnp.var(x, axis=axis, keepdims=True)
    return (x - m) / jnp.sqrt(v + eps)

def _scatter_add(tgt, idx, src, axis=0):
    return tgt.at[idx].add(src)

def _segment_sum(src, seg, n):
    return jax.ops.segment_sum(src, seg, n)
kernel_name = 'mk_conv_seq_d2_conv_nchw512_r4_376f6e'

def setup_inputs(seed: int=0):
    np.random.seed(seed)
    _w = jnp.asarray

    def _rec_inputs():
        import jax
        import jax.numpy as jnp
        _gk = jax.random.key(seed)
        x = -0.000125 + 0.9999 * jax.random.normal(jax.random.fold_in(_gk, 1), (16, 128, 16, 16), jnp.float32)
        return x
    x = _rec_inputs()

    def _L0_conv_setup():
        import jax, jax.numpy as jnp
        import numpy as np
        NUM_TOPK = 25
        key = jax.random.key(seed)
        ks = jax.random.split(key, 8)
        B, C, H, W = (16, 128, 16, 16)
        E, T = (64, 192)
        s = 0.02
        return {'feat': jax.random.normal(ks[0], (B, C, H, W), jnp.float32), 'text_emb': jax.random.normal(ks[1], (T,), jnp.float32), 'density_w': jax.random.normal(ks[2], (C,), jnp.float32) * s, 'density_b': jnp.zeros((), jnp.float32), 'sparse_w': jax.random.normal(ks[3], (E, C), jnp.float32) * s, 'sparse_b': jnp.zeros((E,), jnp.float32), 'text_w': jax.random.normal(ks[4], (E, T), jnp.float32) * s, 'text_b': jnp.zeros((E,), jnp.float32), 'out_w': jax.random.normal(ks[5], (C, E), jnp.float32) * s, 'out_b': jnp.zeros((C,), jnp.float32)}
    _L0_conv_all = _L0_conv_setup()
    _L0_conv_in = {k: v for k, v in _L0_conv_all.items() if k in ('text_emb', 'density_w', 'density_b', 'sparse_w', 'sparse_b', 'text_w', 'text_b', 'out_w', 'out_b')}
    del _L0_conv_all

    def _L1_conv_setup():
        import jax, jax.numpy as jnp
        import numpy as np
        B, C, H, W = (4, 128, 16, 16)
        CQK = C // 8
        key = jax.random.key(seed)
        ks = jax.random.split(key, 8)
        s = 0.05
        return {'x': jax.random.normal(ks[0], (B, C, H, W), dtype=jnp.float32), 'Wq': jax.random.normal(ks[1], (CQK, C), dtype=jnp.float32) * s, 'bq': jax.random.normal(ks[2], (CQK,), dtype=jnp.float32) * s, 'Wk': jax.random.normal(ks[3], (CQK, C), dtype=jnp.float32) * s, 'bk': jax.random.normal(ks[4], (CQK,), dtype=jnp.float32) * s, 'Wv': jax.random.normal(ks[5], (C, C), dtype=jnp.float32) * s, 'bv': jax.random.normal(ks[6], (C,), dtype=jnp.float32) * s, 'gamma': jax.random.normal(ks[7], (1,), dtype=jnp.float32)}
    _L1_conv_all = _L1_conv_setup()
    _L1_conv_in = {k: v for k, v in _L1_conv_all.items() if k in ('Wq', 'bq', 'Wk', 'bk', 'Wv', 'bv', 'gamma')}
    del _L1_conv_all
    return {'x': x, 'L0_conv_text_emb': _L0_conv_in['text_emb'], 'L0_conv_density_w': _L0_conv_in['density_w'], 'L0_conv_density_b': _L0_conv_in['density_b'], 'L0_conv_sparse_w': _L0_conv_in['sparse_w'], 'L0_conv_sparse_b': _L0_conv_in['sparse_b'], 'L0_conv_text_w': _L0_conv_in['text_w'], 'L0_conv_text_b': _L0_conv_in['text_b'], 'L0_conv_out_w': _L0_conv_in['out_w'], 'L0_conv_out_b': _L0_conv_in['out_b'], 'L1_conv_Wq': _L1_conv_in['Wq'], 'L1_conv_bq': _L1_conv_in['bq'], 'L1_conv_Wk': _L1_conv_in['Wk'], 'L1_conv_bk': _L1_conv_in['bk'], 'L1_conv_Wv': _L1_conv_in['Wv'], 'L1_conv_bv': _L1_conv_in['bv'], 'L1_conv_gamma': _L1_conv_in['gamma']}

def reference(x, L0_conv_text_emb, L0_conv_density_w, L0_conv_density_b, L0_conv_sparse_w, L0_conv_sparse_b, L0_conv_text_w, L0_conv_text_b, L0_conv_out_w, L0_conv_out_b, L1_conv_Wq, L1_conv_bq, L1_conv_Wk, L1_conv_bk, L1_conv_Wv, L1_conv_bv, L1_conv_gamma):
    import jax
    import jax.numpy as jnp

    def _L0_conv_ref(feat, text_emb, density_w, density_b, sparse_w, sparse_b, text_w, text_b, out_w, out_b):
        import jax, jax.numpy as jnp
        import numpy as np
        NUM_TOPK = 25
        B, C, H, W = feat.shape
        density = jax.nn.sigmoid(jnp.einsum('bchw,c->bhw', feat, density_w) + density_b).reshape(B, H * W)
        _, topk_idx = jax.lax.top_k(density, NUM_TOPK)
        feat_flat = feat.reshape(B, C, H * W).transpose(0, 2, 1)
        sparse_feat = jnp.take_along_axis(feat_flat, topk_idx[:, :, None], axis=1)
        text_feat = text_w @ text_emb + text_b
        fused = jnp.einsum('bkc,ec->bke', sparse_feat, sparse_w) + sparse_b + text_feat
        fused = jnp.einsum('bke,ce->bkc', fused, out_w) + out_b
        tensor_flat = feat_flat.at[jnp.arange(B)[:, None], topk_idx].set(fused)
        return tensor_flat.transpose(0, 2, 1).reshape(B, C, H, W)

    def _L1_conv_ref(x, Wq, bq, Wk, bk, Wv, bv, gamma):
        import jax, jax.numpy as jnp
        import numpy as np
        B, C, H, W = (4, 128, 16, 16)
        CQK = C // 8
        b, c, h, w = x.shape
        hw = h * w
        q = jnp.einsum('bchw,dc->bdhw', x, Wq) + bq[None, :, None, None]
        k = jnp.einsum('bchw,dc->bdhw', x, Wk) + bk[None, :, None, None]
        v = jnp.einsum('bchw,dc->bdhw', x, Wv) + bv[None, :, None, None]
        q = q.reshape(b, -1, hw)
        k = k.reshape(b, -1, hw)
        v = v.reshape(b, -1, hw)
        attn = jax.nn.softmax(jnp.einsum('bdi,bdj->bij', q, k), axis=-1)
        out = jnp.einsum('bcj,bij->bci', v, attn).reshape(b, c, h, w)
        return gamma[0] * out + x

    def _gn(v, G=32, eps=1e-05):
        B_, C_, H_, W_ = v.shape
        g = v.reshape(B_, G, C_ // G, H_, W_)
        m = jnp.mean(g, axis=(2, 3, 4), keepdims=True)
        s = jnp.var(g, axis=(2, 3, 4), keepdims=True)
        return ((g - m) / jnp.sqrt(s + eps)).reshape(v.shape)

    def _ln_c(v, eps=1e-06):
        m = jnp.mean(v, axis=1, keepdims=True)
        s = jnp.var(v, axis=1, keepdims=True)
        return (v - m) / jnp.sqrt(s + eps)

    def _ln_t(v, eps=1e-05):
        m = jnp.mean(v, axis=-1, keepdims=True)
        s = jnp.var(v, axis=-1, keepdims=True)
        return (v - m) / jnp.sqrt(s + eps)

    def _to_tokens(v):
        B_, C_, H_, W_ = v.shape
        return v.reshape(B_, C_, H_ * W_).transpose(0, 2, 1)

    def _from_tokens(t, like):
        B_, C_, H_, W_ = like.shape
        return t.transpose(0, 2, 1).reshape(B_, C_, H_, W_)
    x = _L0_conv_ref(x, L0_conv_text_emb, L0_conv_density_w, L0_conv_density_b, L0_conv_sparse_w, L0_conv_sparse_b, L0_conv_text_w, L0_conv_text_b, L0_conv_out_w, L0_conv_out_b)
    x = _L1_conv_ref(x, L1_conv_Wq, L1_conv_bq, L1_conv_Wk, L1_conv_bk, L1_conv_Wv, L1_conv_bv, L1_conv_gamma)
    return x

_drawn_inputs = setup_inputs


def setup_inputs(seed=0):
    import zlib

    import numpy as np

    out = dict(_drawn_inputs(seed))
    spreads = {'L0_conv_sparse_b': (0.0, 0.8),
     'L0_conv_text_b': (0.0, 0.8),
     'L0_conv_out_b': (0.0, 0.274)}
    factors = {'L0_conv_text_emb': 4.519,
     'L0_conv_sparse_w': 4.738,
     'L0_conv_text_w': 4.433,
     'L1_conv_Wq': 8.0,
     'L1_conv_bq': 8.0,
     'L1_conv_Wk': 8.0,
     'L1_conv_bk': 8.0,
     'L1_conv_Wv': 8.0,
     'L1_conv_bv': 8.0}
    for name, (base, spread) in spreads.items():
        noise = np.random.default_rng([zlib.crc32(name.encode()), seed]).standard_normal(out[name].shape)
        drawn = base * np.exp(spread * noise) if base else spread * noise
        out[name] = jnp.asarray(drawn.astype(out[name].dtype))
    for name, factor in factors.items():
        out[name] = (out[name] * factor).astype(out[name].dtype)
    return out
```

```python
from contextlib import ExitStack

import concourse.bass as bass
from concourse import mybir
from concourse.alu_op_type import AluOpType as ALU

ACT = mybir.ActivationFunctionType
AX = mybir.AxisListType
F32 = mybir.dt.float32
BF16 = mybir.dt.bfloat16
U32 = mybir.dt.uint32

TOPK = 25
SIGMOID_IS_ONE = 16.635532
SIGMOID_IS_ZERO = -88.72284
TAKEN = -3.0e38

QUERY_PARTS = [0, 0, 1, 1, 0, 2]
KEY_PARTS = [0, 1, 0, 1, 2, 0]


def sparse_fusion_attention(nc, x, text_emb, density_w, density_b, sparse_w, sparse_b, text_w, text_b,
                            out_w, out_b, Wq, bq, Wk, bk, Wv, bv, gamma, out):
    B, C, H, W = x.shape
    HW = H * W
    E, T = text_w.shape
    D = Wq.shape[0]
    QUAD = 32
    GB = 128 // QUAD
    G = B // GB
    PB = 2
    NP = B // PB
    JC = HW // 128
    NS = len(QUERY_PARTS)
    K = NS * D
    HB = B // 2
    VC = C + 1
    assert C == 128 and 2 * D == QUAD and B == G * GB

    parts_dram = nc.dram_tensor("parts_dram", (B // (128 // QUAD), 128, 3, HW), BF16, kind="Internal").ap()
    part_rows = parts_dram.rearrange("g (j s d) t n -> s d (g j) t n", s=2, d=D)
    x_view = x.rearrange("b c h w -> c b (h w)")
    out_view = out.rearrange("b c h w -> c b (h w)")

    with ExitStack() as ctx:
        def sb(name, shape, dt=F32):
            return ctx.enter_context(nc.sbuf_tensor(name, shape, dt))

        def sem(name):
            return ctx.enter_context(nc.semaphore(name))

        bank = [ctx.enter_context(nc.psum_tensor(f"bank{i}", [128, 512], F32)) for i in range(8)]

        tok = sb("tok", [128, B, HW])
        fused = sb("fused", [128, B, HW])
        wqk_raw = sb("wqk_raw", [2 * D, C])
        wv_raw = sb("wv_raw", [C, C])
        outw_raw = sb("outw_raw", [C, E])
        sparse_raw = sb("sparse_raw", [E, C])
        text_raw = sb("text_raw", [E, T])
        emb_rows = sb("emb_rows", [E, T])
        text_prod = sb("text_prod", [E, T])
        e_cols = sb("e_cols", [E, 8])
        c_cols = sb("c_cols", [128, 8])
        bqk = sb("bqk", [128, 1])
        ident = sb("ident", [128, 128])
        wqkT = sb("wqkT", [C, 2 * D])
        wvT = sb("wvT", [C, C])
        outwT = sb("outwT", [E, C])
        fuseT = sb("fuseT", [C, C])
        dens_w = sb("dens_w", [C, G, QUAD])
        key_a = sb("key_a", [128, HW])
        key_b = sb("key_b", [128, HW])
        top8 = sb("top8", [128, 8])
        last8 = sb("last8", [128, 8])
        mask = sb("mask", [128, HW], BF16)
        sel = sb("sel", [128, B, 128], BF16)
        qk = sb("qk", [128, 2, HW])
        rem1 = sb("rem1", [128, 2, HW])
        rem2 = sb("rem2", [128, 2, HW])
        parts = sb("parts", [128, G, 3, HW], BF16)
        q_stack = sb("q_stack", [K, B, HW], BF16)
        k_stack = sb("k_stack", [K, B, HW], BF16)
        val = sb("val", [128, B, JC, VC])
        ones = sb("ones", [128, 128], BF16)
        neg_max = sb("neg_max", [128, 2, JC])
        shift = sb("shift", [128, 2, JC, 128], BF16)
        ew = sb("ew", [128, 2, JC, HW])
        rsum = sb("rsum", [128, 2, JC])
        att = sb("att", [128, 2, JC, C])

        x_in = [sem(f"x_in{i}") for i in range(NP)]
        w_in = sem("w_in")
        v_in = sem("v_in")
        dens_w_zero = sem("dens_w_zero")
        ident_zero = sem("ident_zero")
        ident_ready = sem("ident_ready")
        sel_zero = sem("sel_zero")
        const_ready = sem("const_ready")
        dens_w_ready = sem("dens_w_ready")
        wT_done = sem("wT_done")
        wT_ready = sem("wT_ready")
        fuse_done = sem("fuse_done")
        fuse_ready = sem("fuse_ready")
        text_step = sem("text_step")
        text_ready = sem("text_ready")
        c_done = sem("c_done")
        c_ready = sem("c_ready")
        logits_done = sem("logits_done")
        topk_step = sem("topk_step")
        mask_ready = sem("mask_ready")
        fused_done = sem("fused_done")
        fused_ready = sem("fused_ready")
        bcast_done = sem("bcast_done")
        tok_ready = sem("tok_ready")
        qk_done = sem("qk_done")
        qk_ready = sem("qk_ready")
        p0_ready = sem("p0_ready")
        r1_ready = sem("r1_ready")
        p1_ready = sem("p1_ready")
        r2_ready = sem("r2_ready")
        p2_ready = sem("p2_ready")
        parts_out = [sem(f"parts_out{h}") for h in range(2)]
        stack_in = [sem(f"stack_in{h}") for h in range(2)]
        val_done = sem("val_done")
        val_ready = sem("val_ready")
        s_done = sem("s_done")
        max_ready = sem("max_ready")
        shift_ready = sem("shift_ready")
        st_done = sem("st_done")
        ew_ready = sem("ew_ready")
        att_done = sem("att_done")
        rsum_ready = sem("rsum_ready")
        att_ready = sem("att_ready")
        back_done = sem("back_done")
        res_ready = sem("res_ready")
        stored = sem("stored")

        def row_of(b):
            return QUAD * (b % GB) + b // GB

        W_MATS = 7
        V_VECS = 5 + 2 + 2 * GB

        block = ctx.enter_context(nc.Block())

        @block.sync
        def _(sp):
            for i in range(NP):
                sp.dma_start(tok[:, PB * i:PB * (i + 1), :],
                             x_view[:, PB * i:PB * (i + 1), :]).then_inc(x_in[i], 16)
            for h in range(2):
                for g in range(2 * h, 2 * h + 2):
                    sp.wait_ge(p0_ready, g + 1)
                    sp.wait_ge(p1_ready, g + 1)
                    sp.wait_ge(p2_ready, g + 1)
                    sp.dma_start(parts_dram[g], parts[:, g]).then_inc(parts_out[h], 16)
                sp.wait_ge(parts_out[h], 32)
                for stack, of, s in ((q_stack, QUERY_PARTS, 0), (k_stack, KEY_PARTS, 1)):
                    for r in range(NS):
                        sp.dma_start(stack[D * r:D * (r + 1), HB * h:HB * (h + 1), :],
                                     part_rows[s, :, HB * h:HB * (h + 1), of[r], :]
                                     ).then_inc(stack_in[h], 16)
            with sp.Fori(0, B) as b:
                sp.wait_ge(res_ready, b + 1)
                sp.dma_start(out_view[:, b, :], tok[:, b, :]).then_inc(stored, 16)
            sp.wait_ge(stored, 16 * B)

        @block.gpsimd
        def _(pool):
            pool.memset(ident[:], 0.0).then_inc(ident_zero, 1)
            pool.wait_ge(ident_zero, 1)
            pool.affine_select(out=ident[:], in_=ident[:], compare_op=ALU.not_equal, fill=1.0, base=0,
                               pattern=[[-1, 128]], channel_multiplier=1).then_inc(ident_ready, 1)
            pool.memset(sel[:], 0.0).then_inc(sel_zero, 1)
            pool.wait_ge(sel_zero, 1)
            sel_view = sel[:].rearrange("p (g j) n -> p g j n", j=GB)
            pool.affine_select(out=sel_view, in_=sel_view, compare_op=ALU.not_equal, fill=1.0, base=0,
                               pattern=[[-1, G], [-QUAD, GB], [0, 128]], channel_multiplier=1)
            pool.memset(ones[:], 1.0)
            pool.memset(val[:, :, :, C:VC], 1.0).then_inc(const_ready, 1)
            for g in range(G):
                s = g % 2
                pool.wait_ge(p0_ready, g + 1)
                if g >= 2:
                    pool.wait_ge(r2_ready, g - 1)
                pool.tensor_tensor(rem1[:, s, :], qk[:, s, :], parts[:, g, 0, :], ALU.subtract
                                   ).then_inc(r1_ready, 1)
                pool.wait_ge(p1_ready, g + 1)
                if g >= 2:
                    pool.wait_ge(p2_ready, g - 1)
                pool.tensor_tensor(rem2[:, s, :], rem1[:, s, :], parts[:, g, 1, :], ALU.subtract
                                   ).then_inc(r2_ready, 1)

            def shift_step(b, s, reused):
                pool.wait_ge(max_ready, b + 1)
                if reused:
                    pool.wait_ge(st_done, b - 1)
                pool.tensor_tensor(shift[:, s], ident[:].unsqueeze(1).to_broadcast([128, JC, 128]),
                                   neg_max[:, s, :].unsqueeze(2).to_broadcast([128, JC, 128]),
                                   ALU.mult).then_inc(shift_ready, 1)

            shift_step(0, 0, False)
            shift_step(1, 1, False)
            with pool.Fori(1, B // 2) as i:
                shift_step(2 * i, 0, True)
                shift_step(2 * i + 1, 1, True)

        @block.scalar
        def _(act):
            for dst, src in ((c_cols[:, 0:1], density_w.rearrange("(c o) -> c o", o=1)),
                             (outw_raw[:], out_w), (sparse_raw[:], sparse_w),
                             (wqk_raw[0:D, :], Wq), (wqk_raw[D:2 * D, :], Wk),
                             (wv_raw[:], Wv), (text_raw[:], text_w)):
                act.dma_start(dst, src).then_inc(w_in, 16)
            act.dma_start(emb_rows[:], text_emb.rearrange("(o t) -> o t", o=1).to_broadcast([E, T])
                          ).then_inc(v_in, 16)
            for dst, src in ((e_cols[:, 0:1], sparse_b), (e_cols[:, 1:2], text_b), (c_cols[:, 2:3], out_b),
                             (c_cols[:, 3:4], bv)):
                act.dma_start(dst, src.rearrange("(c o) -> c o", o=1)).then_inc(v_in, 16)
            act.dma_start(c_cols[:, 4:5], gamma.rearrange("(o t) -> o t", o=1).to_broadcast([C, 1])
                          ).then_inc(v_in, 16)
            act.dma_start(c_cols[:, 1:2], density_b.rearrange("(o t) -> o t", o=1).to_broadcast([C, 1])
                          ).then_inc(v_in, 16)
            for j in range(GB):
                for first, vec in ((0, bq), (D, bk)):
                    act.dma_start(bqk[QUAD * j + first:QUAD * j + first + D, :],
                                  vec.rearrange("(c o) -> c o", o=1)).then_inc(v_in, 16)
            act.wait_ge(c_done, 1)
            act.wait_ge(v_in, 16 * (V_VECS))
            act.activation(c_cols[:, 5:6], bank[6][:, 0:1], ACT.Identity, bias=c_cols[:, 2:3]
                           ).then_inc(c_ready, 1)
            act.wait_ge(c_ready, 1)
            for i in range(NP):
                act.wait_ge(fused_done, i + 1)
                act.activation(fused[:, PB * i:PB * (i + 1), :],
                               bank[1 + i % 2][:].rearrange("p (b n) -> p b n", b=PB),
                               ACT.Identity, bias=c_cols[:, 5:6]).then_inc(fused_ready, 1)
            for g in range(G):
                act.wait_ge(qk_done, g + 1)
                if g >= 2:
                    act.wait_ge(r1_ready, g - 1)
                act.activation(qk[:, g % 2, :], bank[5 + g % 2][:, 0:HW], ACT.Identity, bias=bqk[:, 0:1]
                               ).then_inc(qk_ready, 1)
                for i in range(2 * g, 2 * g + 2):
                    act.wait_ge(val_done, i + 1)
                    if i == 0:
                        act.wait_ge(const_ready, 1)
                    act.copy(val[:, PB * i:PB * (i + 1), :, 0:C],
                             bank[7 * (1 - i % 2)][:].rearrange("p (b j n) -> p b j n", b=PB, j=JC)
                             ).then_inc(val_ready, 1)

            def exp_step(b, s, reused):
                act.wait_ge(st_done, b + 1)
                if reused:
                    act.wait_ge(att_done, b - 1)
                act.activation(ew[:, s], bank[3 + s][:].rearrange("p (j n) -> p j n", j=JC), ACT.Exp
                               ).then_inc(ew_ready, 1)

            exp_step(0, 0, False)
            exp_step(1, 1, False)
            with act.Fori(1, B // 2) as i:
                exp_step(2 * i, 0, True)
                exp_step(2 * i + 1, 1, True)

        @block.vector
        def _(dve):
            dve.memset(dens_w[:], 0.0).then_inc(dens_w_zero, 1)
            dve.wait_ge(dens_w_zero, 1)
            dve.wait_ge(w_in, 16 * W_MATS)
            for g in range(G):
                last = dve.tensor_copy(dens_w[:, g, g:g + 1], c_cols[:, 0:1])
            last.then_inc(dens_w_ready, 1)
            dve.wait_ge(wT_done, 1)
            dve.tensor_copy(outwT[:], bank[7][0:E, 0:C])
            dve.tensor_copy(wqkT[:], bank[7][:, 128:128 + 2 * D])
            dve.wait_ge(v_in, 16 * V_VECS)
            dve.tensor_scalar(wvT[:], bank[7][:, 256:256 + C], c_cols[:, 4:5], None, ALU.mult
                              ).then_inc(wT_ready, 1)
            dve.tensor_tensor(text_prod[:], text_raw[:], emb_rows[:], ALU.mult).then_inc(text_step, 1)
            dve.wait_ge(text_step, 1)
            dve.tensor_reduce(e_cols[:, 2:3], text_prod[:], axis=AX.X, op=ALU.add).then_inc(text_step, 1)
            dve.wait_ge(text_step, 2)
            dve.tensor_scalar(e_cols[:, 3:4], e_cols[:, 2:3], e_cols[:, 0:1], e_cols[:, 1:2],
                              ALU.add, ALU.add).then_inc(text_ready, 1)
            dve.tensor_tensor(c_cols[:, 6:7], c_cols[:, 3:4], c_cols[:, 4:5], ALU.mult)
            dve.wait_ge(fuse_done, 1)
            dve.tensor_copy(fuseT[:], bank[6][:, 128:256]).then_inc(fuse_ready, 1)

            steps = [0]

            def chain(ins):
                steps[0] += 1
                ins.then_inc(topk_step, 1)
                dve.wait_ge(topk_step, steps[0])

            chain(dve.memset(last8[:], TAKEN))
            dve.wait_ge(logits_done, 1)
            chain(dve.tensor_scalar(key_b[:], bank[0][:, 0:HW], c_cols[:, 1:2], SIGMOID_IS_ONE,
                                    ALU.add, ALU.min))
            chain(dve.tensor_scalar(key_a[:], key_b[:], SIGMOID_IS_ZERO, None, ALU.max))
            keys, free = key_a, key_b
            for _ in range(TOPK // 8):
                chain(dve.max(top8[:], keys[:]))
                chain(dve.match_replace(out=free[:], in_to_replace=top8[:], in_values=keys[:],
                                        imm_value=TAKEN))
                keys, free = free, keys
            chain(dve.max(top8[:], keys[:]))
            chain(dve.tensor_copy(last8[:, 0:TOPK % 8], top8[:, 0:TOPK % 8]))
            chain(dve.match_replace(out=free[:], in_to_replace=last8[:], in_values=keys[:],
                                    imm_value=TAKEN))
            dve.tensor_scalar(mask[:], free[:], TAKEN, None, ALU.is_equal).then_inc(mask_ready, 1)

            def token_step(i):
                pair = slice(PB * i, PB * (i + 1))
                dve.wait_ge(fused_ready, i + 1)
                dve.wait_ge(bcast_done, i + 1)
                dve.copy_predicated(tok[:, pair, :],
                                    bank[3 + i % 2][:].rearrange("p (b n) -> p b n", b=PB).bitcast(U32),
                                    fused[:, pair, :]).then_inc(tok_ready, 1)

            def part_steps(g):
                s = g % 2
                dve.wait_ge(qk_ready, g + 1)
                dve.tensor_copy(parts[:, g, 0, :], qk[:, s, :]).then_inc(p0_ready, 1)
                dve.wait_ge(r1_ready, g + 1)
                dve.tensor_copy(parts[:, g, 1, :], rem1[:, s, :]).then_inc(p1_ready, 1)
                dve.wait_ge(r2_ready, g + 1)
                dve.tensor_copy(parts[:, g, 2, :], rem2[:, s, :]).then_inc(p2_ready, 1)

            for g in range(G):
                token_step(2 * g)
                token_step(2 * g + 1)
                if g >= 1:
                    part_steps(g - 1)
            part_steps(G - 1)

            def max_step(b, s):
                dve.wait_ge(s_done, b + 1)
                dve.tensor_reduce(neg_max[:, s, :], bank[1 + s][:].rearrange("p (c n) -> p c n", c=JC),
                                  axis=AX.X, op=ALU.max, negate=True).then_inc(max_ready, 1)

            def norm_step(b, s):
                o = bank[5 + s][:].rearrange("p (c n) -> p c n", c=JC)
                dve.wait_ge(att_done, b + 1)
                dve.reciprocal(rsum[:, s, :], o[:, :, C]).then_inc(rsum_ready, 1)
                dve.wait_ge(rsum_ready, b + 1)
                dve.tensor_tensor(att[:, s], o[:, :, 0:C],
                                  rsum[:, s, :].unsqueeze(2).to_broadcast([128, JC, C]),
                                  ALU.mult).then_inc(att_ready, 1)

            def result_step(b, s):
                dve.wait_ge(back_done, b + 1)
                dve.scalar_tensor_tensor(out=tok[:, b, :], in0=bank[7 * (1 - s)][:, 0:HW],
                                         scalar=c_cols[:, 6:7], in1=tok[:, b, :],
                                         op0=ALU.add, op1=ALU.add).then_inc(res_ready, 1)

            max_step(0, 0)
            max_step(1, 1)
            max_step(2, 0)
            norm_step(0, 0)
            max_step(3, 1)
            result_step(0, 0)
            norm_step(1, 1)
            with dve.Fori(1, B // 2 - 1) as i:
                for s in range(2):
                    b = 2 * i + s
                    max_step(b + 2, s)
                    result_step(b - 1, 1 - s)
                    norm_step(b, s)
            for b in range(B - 2, B):
                result_step(b - 1, (b - 1) % 2)
                norm_step(b, b % 2)
            result_step(B - 1, (B - 1) % 2)

        @block.tensor
        def _(pe):
            pe.wait_ge(ident_ready, 1)
            pe.wait_ge(w_in, 16 * W_MATS)
            pe.transpose(bank[7][0:E, 0:C], outw_raw[:], ident[:])
            pe.transpose(bank[7][:, 128:128 + 2 * D], wqk_raw[:], ident[0:2 * D, 0:2 * D])
            pe.transpose(bank[7][:, 256:256 + C], wv_raw[:], ident[:]).then_inc(wT_done, 1)

            pe.wait_ge(dens_w_ready, 1)

            def density(g):
                for j in range(GB):
                    if j % PB == 0:
                        pe.wait_ge(x_in[(GB * g + j) // PB], 16)
                    last = pe.matmul(bank[0][QUAD * j:QUAD * (j + 1), 0:HW], dens_w[:, g, :],
                                     tok[:, GB * g + j, :], start=g == 0, stop=g == G - 1)
                if g == G - 1:
                    last.then_inc(logits_done, 1)

            def fuse(i):
                if i >= 2:
                    pe.wait_ge(fused_ready, i - 1)
                pe.matmul(bank[1 + i % 2][:], fuseT[:], tok[:, PB * i:PB * (i + 1), :].rearrange("p b n -> p (b n)"),
                          start=True, stop=True).then_inc(fused_done, 1)

            density(0)
            pe.wait_ge(wT_ready, 1)
            pe.matmul(bank[6][:, 128:128 + C], sparse_raw[:], outwT[:], start=True, stop=True
                      ).then_inc(fuse_done, 1)
            pe.wait_ge(fuse_ready, 1)
            pe.wait_ge(text_ready, 1)
            pe.matmul(bank[6][:, 0:1], outwT[:], e_cols[:, 3:4], start=True, stop=True).then_inc(c_done, 1)
            for g in range(1, G):
                density(g)
            for i in range(NP):
                fuse(i)

            pe.wait_ge(mask_ready, 1)
            pe.wait_ge(const_ready, 1)

            def broadcast(i):
                if i >= 2:
                    pe.wait_ge(tok_ready, i - 1)
                for b in range(PB * i, PB * (i + 1)):
                    last = pe.matmul(bank[3 + i % 2][:, HW * (b % PB):HW * (b % PB + 1)], sel[:, b, :],
                                     mask[:], start=True, stop=True)
                last.then_inc(bcast_done, 1)

            def project(g):
                if g >= 2:
                    pe.wait_ge(qk_ready, g - 1)
                if g == 1:
                    pe.wait_ge(c_ready, 1)
                for j in range(GB):
                    if j % PB == 0:
                        pe.wait_ge(tok_ready, (GB * g + j) // PB + 1)
                    last = pe.matmul(bank[5 + g % 2][QUAD * j:QUAD * (j + 1), 0:HW], wqkT[:],
                                     tok[:, GB * g + j, :], start=True, stop=True)
                last.then_inc(qk_done, 1)
                for i in range(2 * g, 2 * g + 2):
                    if i >= 2:
                        pe.wait_ge(val_ready, i - 1)
                    for c in range(PB * JC):
                        last = pe.matmul(bank[7 * (1 - i % 2)][:, 128 * c:128 * (c + 1)],
                                         tok[:, PB * i + c // JC, 128 * (c % JC):128 * (c % JC + 1)],
                                         wvT[:], start=True, stop=True)
                    last.then_inc(val_done, 1)

            broadcast(0)
            broadcast(1)
            for g in range(G):
                if g + 1 < G:
                    broadcast(2 * g + 2)
                    broadcast(2 * g + 3)
                project(g)

            def scores(b, s):
                for c in range(JC):
                    last = pe.matmul(bank[1 + s][:, HW * c:HW * (c + 1)],
                                     q_stack[:, b, 128 * c:128 * (c + 1)], k_stack[:, b, :],
                                     start=True, stop=True)
                last.then_inc(s_done, 1)

            def scores_transposed(b, s, reused):
                pe.wait_ge(shift_ready, b + 1)
                if reused:
                    pe.wait_ge(ew_ready, b - 1)
                sh = shift[:, s].rearrange("p c n -> p (c n)")
                pe.matmul(bank[3 + s][:], ones[:], sh.unsqueeze(1).to_broadcast([128, JC, HW]),
                          start=True, stop=False)
                for c in range(JC):
                    last = pe.matmul(bank[3 + s][:, HW * c:HW * (c + 1)],
                                     k_stack[:, b, 128 * c:128 * (c + 1)], q_stack[:, b, :],
                                     start=False, stop=c == JC - 1)
                last.then_inc(st_done, 1)

            def attend(b, s, reused):
                pe.wait_ge(ew_ready, b + 1)
                if reused:
                    pe.wait_ge(att_ready, b - 1)
                for c in range(JC):
                    for j in range(JC):
                        last = pe.matmul(bank[5 + s][:, HW * c:HW * c + VC],
                                         ew[:, s, j, 128 * c:128 * (c + 1)], val[:, b, j, :],
                                         start=j == 0, stop=j == JC - 1)
                last.then_inc(att_done, 1)

            def back(b, s, reused):
                pe.wait_ge(att_ready, b + 1)
                if reused:
                    pe.wait_ge(res_ready, b - 1)
                for c in range(JC):
                    last = pe.transpose(bank[7 * (1 - s)][:, 128 * c:128 * (c + 1)], att[:, s, c, :],
                                        ident[:])
                last.then_inc(back_done, 1)

            for h in range(2):
                pe.wait_ge(stack_in[h], 16 * 2 * NS)
            pe.wait_ge(fused_ready, NP)
            scores(0, 0)
            scores(1, 1)
            scores_transposed(0, 0, False)
            pe.wait_ge(qk_ready, G)
            pe.wait_ge(val_ready, NP)
            for b in range(2):
                scores_transposed(b + 1, (b + 1) % 2, b >= 1)
                scores(b + 2, b % 2)
                if b >= 1:
                    back(b - 1, (b - 1) % 2, False)
                attend(b, b % 2, False)
            with pe.Fori(1, B // 2 - 1) as i:
                for s in range(2):
                    b = 2 * i + s
                    scores_transposed(b + 1, 1 - s, True)
                    scores(b + 2, s)
                    back(b - 1, 1 - s, True)
                    attend(b, s, True)
            scores_transposed(B - 1, 1, True)
            back(B - 3, (B - 3) % 2, True)
            attend(B - 2, 0, True)
            back(B - 2, 0, True)
            attend(B - 1, 1, True)
            back(B - 1, 1, True)


_INS = ['x', 'L0_conv_text_emb', 'L0_conv_density_w', 'L0_conv_density_b', 'L0_conv_sparse_w',
        'L0_conv_sparse_b', 'L0_conv_text_w', 'L0_conv_text_b', 'L0_conv_out_w', 'L0_conv_out_b',
        'L1_conv_Wq', 'L1_conv_bq', 'L1_conv_Wk', 'L1_conv_bk', 'L1_conv_Wv', 'L1_conv_bv',
        'L1_conv_gamma']
_OUTS = [((16, 128, 16, 16), 'float32')]


def kernel(**inputs):
    import numpy as _np
    import concourse.bacc as _bacc
    from concourse import mybir as _mybir
    from concourse.bass_utils import run_bass_kernel_spmd as _run

    nc = _bacc.Bacc("TRN2", target_bir_lowering=False, num_devices=1)
    arrays, args = {}, []
    for name in _INS:
        a = _np.ascontiguousarray(inputs[name])
        if a.ndim == 0 or name == 'L0_conv_density_b':
            a = a.reshape(1)
        arrays[f"in_{name}_dram"] = a
        args.append(nc.dram_tensor(f"in_{name}_dram", a.shape, _mybir.dt.from_np(a.dtype), kind="ExternalInput").ap())
    for i, (shape, dtype) in enumerate(_OUTS):
        dt = _mybir.dt.from_np(_np.dtype(dtype))
        args.append(nc.dram_tensor(f"out_{i}_dram", shape, dt, kind="ExternalOutput").ap())
    sparse_fusion_attention(nc, *args)
    r = _run(nc, [arrays], core_ids=[0])
    got = tuple(r.results[0][f"out_{i}_dram"] for i in range(len(_OUTS)))
    return got[0]
```

```python
from contextlib import ExitStack

import concourse.bass as bass
from concourse import mybir
from concourse.alu_op_type import AluOpType as ALU

ACT = mybir.ActivationFunctionType
AX = mybir.AxisListType
F32 = mybir.dt.float32
BF16 = mybir.dt.bfloat16
U32 = mybir.dt.uint32

TOPK = 25
SIGMOID_IS_ONE = 16.635532
SIGMOID_IS_ZERO = -88.72284
TAKEN = -3.0e38

QUERY_PARTS = [0, 0, 1, 1, 0, 2]
KEY_PARTS = [0, 1, 0, 1, 2, 0]


def parameter_columns(C, E, T, D):
    widths = [("density_w", 1), ("density_b", 1), ("gamma", 1), ("bv", 1), ("out_b", 1), ("bqk", 1),
              ("wvT", C), ("wqkT", 2 * D), ("outwT", C), ("sparse_w", C), ("sparse_b", 1), ("text_b", 1),
              ("text_wT", 2 * E), ("emb", 2)]
    at, columns = 0, {}
    for name, width in widths:
        columns[name] = slice(at, at + width)
        at += width
    return columns, at


def sparse_fusion_attention(nc, x, params, E, T, D, out):
    B, C, H, W = x.shape
    HW = H * W
    QUAD = 32
    GB = 128 // QUAD
    G = B // GB
    PB = 2
    NP = B // PB
    JC = HW // 128
    NS = len(QUERY_PARTS)
    K = NS * D
    HB = B // 2
    VC = C + 1
    assert C == 128 and 2 * D == QUAD and B == G * GB

    COLS, PAR_COLS = parameter_columns(C, E, T, D)
    PAR_EARLY = COLS["outwT"].start

    parts_dram = nc.dram_tensor("parts_dram", (B // (128 // QUAD), 128, 3, HW), BF16, kind="Internal").ap()
    part_rows = parts_dram.rearrange("g (j s d) t n -> s d (g j) t n", s=2, d=D)
    x_view = x.rearrange("b c h w -> c b (h w)")
    out_view = out.rearrange("b c h w -> c b (h w)")

    with ExitStack() as ctx:
        def sb(name, shape, dt=F32):
            return ctx.enter_context(nc.sbuf_tensor(name, shape, dt))

        def sem(name):
            return ctx.enter_context(nc.semaphore(name))

        bank = [ctx.enter_context(nc.psum_tensor(f"bank{i}", [128, 512], F32)) for i in range(8)]

        def block_of(name, rows):
            return par[0:rows, COLS[name]]

        tok = sb("tok", [128, B, HW])
        fused = sb("fused", [128, B, HW])
        par = sb("par", [128, PAR_COLS])
        density_w_col, density_b_col = block_of("density_w", C), block_of("density_b", 128)
        gamma_col, bv_col, out_b_col = block_of("gamma", C), block_of("bv", C), block_of("out_b", C)
        bqk_col = block_of("bqk", 128)
        wvT_raw, wqkT, outwT = block_of("wvT", C), block_of("wqkT", C), block_of("outwT", E)
        sparse_rows = block_of("sparse_w", E)
        sparse_b_col, text_b_col = block_of("sparse_b", E), block_of("text_b", E)
        text_wT, emb_cols = block_of("text_wT", T // 2), block_of("emb", T // 2)
        wvT = sb("wvT", [C, C])
        gbv = sb("gbv", [C, 1])
        fuseT = sb("fuseT", [C, C])
        e_sum = sb("e_sum", [E, 1])
        c_col = sb("c_col", [C, 1])
        dens_w = sb("dens_w", [C, 2, QUAD])
        ident = sb("ident", [128, 128])
        key_a = sb("key_a", [128, 2, HW])
        key_b = sb("key_b", [128, 2, HW])
        top8 = sb("top8", [128, 8])
        last8 = sb("last8", [128, 8])
        mask = sb("mask", [128, 2, HW], BF16)
        sel = sb("sel", [128, HB, 128], BF16)
        qk = sb("qk", [128, 2, HW])
        rem1 = sb("rem1", [128, 2, HW])
        parts = sb("parts", [128, G, 3, HW], BF16)
        q_stack = sb("q_stack", [K, B, HW], BF16)
        k_stack = sb("k_stack", [K, B, HW], BF16)
        val = sb("val", [128, B, JC, VC])
        ones = sb("ones", [128, 128], BF16)
        neg_max = sb("neg_max", [128, 2, JC])
        shift = sb("shift", [128, 2, JC, 128], BF16)
        ew = sb("ew", [128, 2, JC, HW])
        rsum = sb("rsum", [128, 2, JC])
        att = sb("att", [128, 2, JC, C])

        x_in = [sem(f"x_in{i}") for i in range(NP)]
        par_in = [sem("par_in0"), sem("par_in1")]
        dens_w_zero = sem("dens_w_zero")
        dens_w_ready = sem("dens_w_ready")
        ident_zero = sem("ident_zero")
        ident_ready = sem("ident_ready")
        sel_zero = sem("sel_zero")
        const_ready = sem("const_ready")
        wvT_ready = sem("wvT_ready")
        fuse_done = sem("fuse_done")
        fuse_ready = sem("fuse_ready")
        text_done = sem("text_done")
        text_ready = sem("text_ready")
        c_done = sem("c_done")
        c_ready = sem("c_ready")
        logits_done = sem("logits_done")
        keys_ready = sem("keys_ready")
        topk_step = sem("topk_step")
        mask_ready = sem("mask_ready")
        fused_done = sem("fused_done")
        fused_ready = sem("fused_ready")
        bcast_done = sem("bcast_done")
        tok_ready = sem("tok_ready")
        qk_done = sem("qk_done")
        qk_ready = sem("qk_ready")
        p0_ready = sem("p0_ready")
        r1_ready = sem("r1_ready")
        p1_ready = sem("p1_ready")
        p2_ready = sem("p2_ready")
        parts_out = [sem(f"parts_out{h}") for h in range(2)]
        stack_in = [sem(f"stack_in{h}") for h in range(2)]
        val_done = sem("val_done")
        val_ready = sem("val_ready")
        s_done = sem("s_done")
        max_ready = sem("max_ready")
        shift_ready = sem("shift_ready")
        st_done = sem("st_done")
        ew_ready = sem("ew_ready")
        att_done = sem("att_done")
        rsum_ready = sem("rsum_ready")
        att_ready = sem("att_ready")
        back_done = sem("back_done")
        res_ready = sem("res_ready")
        stored = sem("stored")

        block = ctx.enter_context(nc.Block())

        @block.sync
        def _(sp):
            sp.dma_start(par[:, 0:PAR_EARLY], params[:, 0:PAR_EARLY]).then_inc(par_in[0], 16)
            for i in range(NP):
                sp.dma_start(tok[:, PB * i:PB * (i + 1), :],
                             x_view[:, PB * i:PB * (i + 1), :]).then_inc(x_in[i], 16)
                if i == 0:
                    sp.dma_start(par[:, PAR_EARLY:], params[:, PAR_EARLY:]).then_inc(par_in[1], 16)
            for h in range(2):
                for g in range(2 * h, 2 * h + 2):
                    sp.wait_ge(p0_ready, g + 1)
                    sp.wait_ge(p1_ready, g + 1)
                    sp.wait_ge(p2_ready, g + 1)
                    sp.dma_start(parts_dram[g], parts[:, g]).then_inc(parts_out[h], 16)
                sp.wait_ge(parts_out[h], 32)
                for stack, of, s in ((q_stack, QUERY_PARTS, 0), (k_stack, KEY_PARTS, 1)):
                    for r in range(NS):
                        sp.dma_start(stack[D * r:D * (r + 1), HB * h:HB * (h + 1), :],
                                     part_rows[s, :, HB * h:HB * (h + 1), of[r], :]
                                     ).then_inc(stack_in[h], 16)
            with sp.Fori(0, B) as b:
                sp.wait_ge(res_ready, b + 1)
                sp.dma_start(out_view[:, b, :], tok[:, b, :]).then_inc(stored, 16)
            sp.wait_ge(stored, 16 * B)

        @block.gpsimd
        def _(pool):
            pool.memset(sel[:], 0.0).then_inc(sel_zero, 1)
            pool.wait_ge(sel_zero, 1)
            sel_view = sel[:].rearrange("p (g j) n -> p g j n", j=GB)
            pool.affine_select(out=sel_view, in_=sel_view, compare_op=ALU.not_equal, fill=1.0, base=0,
                               pattern=[[-1, 2], [-QUAD, GB], [0, 128]], channel_multiplier=1)
            pool.memset(ones[:], 1.0)
            pool.memset(val[:, :, :, C:VC], 1.0).then_inc(const_ready, 1)
            pool.memset(ident[:], 0.0).then_inc(ident_zero, 1)
            pool.wait_ge(ident_zero, 1)
            pool.affine_select(out=ident[:], in_=ident[:], compare_op=ALU.not_equal, fill=1.0, base=0,
                               pattern=[[-1, 128]], channel_multiplier=1).then_inc(ident_ready, 1)
            for g in range(G):
                s = g % 2
                pool.wait_ge(p0_ready, g + 1)
                pool.tensor_tensor(rem1[:, s, :], qk[:, s, :], parts[:, g, 0, :], ALU.subtract
                                   ).then_inc(r1_ready, 1)
                pool.wait_ge(p1_ready, g + 1)
                pool.tensor_tensor(parts[:, g, 2, :], rem1[:, s, :], parts[:, g, 1, :], ALU.subtract
                                   ).then_inc(p2_ready, 1)

            def shift_step(b, s, reused):
                pool.wait_ge(max_ready, b + 1)
                if reused:
                    pool.wait_ge(st_done, b - 1)
                pool.tensor_tensor(shift[:, s], ident[:].unsqueeze(1).to_broadcast([128, JC, 128]),
                                   neg_max[:, s, :].unsqueeze(2).to_broadcast([128, JC, 128]),
                                   ALU.mult).then_inc(shift_ready, 1)

            pool.wait_ge(ident_ready, 1)
            shift_step(0, 0, False)
            shift_step(1, 1, False)
            with pool.Fori(1, B // 2) as i:
                shift_step(2 * i, 0, True)
                shift_step(2 * i + 1, 1, True)

        @block.scalar
        def _(act):
            act.wait_ge(par_in[0], 16)
            act.wait_ge(c_done, 1)
            act.activation(c_col[:], bank[7][:, 0:1], ACT.Identity, bias=out_b_col).then_inc(c_ready, 1)
            act.wait_ge(c_ready, 1)

            def fused_out(i):
                act.wait_ge(fused_done, i + 1)
                act.activation(fused[:, PB * i:PB * (i + 1), :],
                               bank[1 + i % 2][:].rearrange("p (b n) -> p b n", b=PB),
                               ACT.Identity, bias=c_col[:]).then_inc(fused_ready, 1)

            def qk_out(g):
                act.wait_ge(qk_done, g + 1)
                if g >= 2:
                    act.wait_ge(r1_ready, g - 1)
                act.activation(parts[:, g, 0, :], bank[5 + g % 2][:, 0:HW], ACT.Identity, bias=bqk_col)
                act.activation(qk[:, g % 2, :], bank[5 + g % 2][:, 0:HW], ACT.Identity, bias=bqk_col
                               ).then_inc(p0_ready, 1)

            def val_out(i):
                act.wait_ge(val_done, i + 1)
                act.copy(val[:, PB * i:PB * (i + 1), :, 0:C],
                         bank[7 * (1 - i % 2)][:].rearrange("p (b j n) -> p b j n", b=PB, j=JC)
                         ).then_inc(val_ready, 1)

            for i in range(NP):
                fused_out(i)
            act.wait_ge(const_ready, 1)
            for h in range(2):
                for g in range(2 * h, 2 * h + 2):
                    qk_out(g)
                for i in range(NP // 2 * h, NP // 2 * (h + 1)):
                    val_out(i)

            def exp_step(b, s, reused):
                act.wait_ge(st_done, b + 1)
                if reused:
                    act.wait_ge(att_done, b - 1)
                act.activation(ew[:, s], bank[3 + s][:].rearrange("p (j n) -> p j n", j=JC), ACT.Exp
                               ).then_inc(ew_ready, 1)

            exp_step(0, 0, False)
            exp_step(1, 1, False)
            with act.Fori(1, B // 2) as i:
                exp_step(2 * i, 0, True)
                exp_step(2 * i + 1, 1, True)

        @block.vector
        def _(dve):
            steps = [0]

            def chain(ins):
                steps[0] += 1
                ins.then_inc(topk_step, 1)
                dve.wait_ge(topk_step, steps[0])

            dve.memset(dens_w[:], 0.0).then_inc(dens_w_zero, 1)
            dve.memset(last8[:], TAKEN)
            dve.wait_ge(dens_w_zero, 1)
            dve.wait_ge(par_in[0], 16)
            for g in range(2):
                last = dve.tensor_copy(dens_w[:, g, g:g + 1], density_w_col)
            last.then_inc(dens_w_ready, 1)
            dve.tensor_scalar(wvT[:], wvT_raw, gamma_col, None, ALU.mult)
            dve.tensor_tensor(gbv[:], bv_col, gamma_col, ALU.mult).then_inc(wvT_ready, 1)
            dve.wait_ge(par_in[1], 16)
            dve.wait_ge(text_done, 1)
            dve.tensor_scalar(e_sum[:], bank[7][0:E, 0:1], sparse_b_col, text_b_col, ALU.add, ALU.add
                              ).then_inc(text_ready, 1)
            dve.wait_ge(fuse_done, 1)
            dve.tensor_copy(fuseT[:], bank[6][:, 0:C]).then_inc(fuse_ready, 1)

            def keys_out(h):
                dve.wait_ge(logits_done, h + 1)
                chain(dve.tensor_scalar(key_b[:, h], bank[5 * h][:, 0:HW], density_b_col, SIGMOID_IS_ONE,
                                        ALU.add, ALU.min))
                dve.tensor_scalar(key_a[:, h], key_b[:, h], SIGMOID_IS_ZERO, None, ALU.max
                                  ).then_inc(keys_ready, 1)
                dve.wait_ge(keys_ready, h + 1)

            def top_k(h):
                keys, free = key_a[:, h], key_b[:, h]
                for _ in range(TOPK // 8):
                    chain(dve.max(top8[:], keys))
                    chain(dve.match_replace(out=free, in_to_replace=top8[:], in_values=keys,
                                            imm_value=TAKEN))
                    keys, free = free, keys
                chain(dve.max(top8[:], keys))
                chain(dve.tensor_copy(last8[:, 0:TOPK % 8], top8[:, 0:TOPK % 8]))
                chain(dve.match_replace(out=free, in_to_replace=last8[:], in_values=keys,
                                        imm_value=TAKEN))
                dve.tensor_scalar(mask[:, h], free, TAKEN, None, ALU.is_equal).then_inc(mask_ready, 1)

            def token_step(i):
                pair = slice(PB * i, PB * (i + 1))
                dve.wait_ge(fused_ready, i + 1)
                dve.wait_ge(bcast_done, i + 1)
                dve.copy_predicated(tok[:, pair, :],
                                    bank[3 + i % 2][:].rearrange("p (b n) -> p b n", b=PB).bitcast(U32),
                                    fused[:, pair, :]).then_inc(tok_ready, 1)

            def second_part(g):
                dve.wait_ge(r1_ready, g + 1)
                if g >= 2:
                    dve.wait_ge(p2_ready, g - 1)
                dve.tensor_copy(parts[:, g, 1, :], rem1[:, g % 2, :]).then_inc(p1_ready, 1)

            keys_out(0)
            top_k(0)
            keys_out(1)
            for i in range(NP // 2):
                token_step(i)
            second_part(0)
            second_part(1)
            top_k(1)
            for i in range(NP // 2, NP):
                token_step(i)
            second_part(2)
            second_part(3)

            def max_step(b, s):
                dve.wait_ge(s_done, b + 1)
                dve.tensor_reduce(neg_max[:, s, :], bank[1 + s][:].rearrange("p (c n) -> p c n", c=JC),
                                  axis=AX.X, op=ALU.max, negate=True).then_inc(max_ready, 1)

            def norm_step(b, s):
                o = bank[5 + s][:].rearrange("p (c n) -> p c n", c=JC)
                dve.wait_ge(att_done, b + 1)
                dve.reciprocal(rsum[:, s, :], o[:, :, C]).then_inc(rsum_ready, 1)
                dve.wait_ge(rsum_ready, b + 1)
                dve.tensor_tensor(att[:, s], o[:, :, 0:C],
                                  rsum[:, s, :].unsqueeze(2).to_broadcast([128, JC, C]),
                                  ALU.mult).then_inc(att_ready, 1)

            def result_step(b, s):
                dve.wait_ge(back_done, b + 1)
                dve.scalar_tensor_tensor(out=tok[:, b, :], in0=bank[7 * (1 - s)][:, 0:HW],
                                         scalar=gbv[:], in1=tok[:, b, :],
                                         op0=ALU.add, op1=ALU.add).then_inc(res_ready, 1)

            dve.wait_ge(wvT_ready, 1)
            max_step(0, 0)
            max_step(1, 1)
            max_step(2, 0)
            norm_step(0, 0)
            max_step(3, 1)
            result_step(0, 0)
            norm_step(1, 1)
            with dve.Fori(1, B // 2 - 1) as i:
                for s in range(2):
                    b = 2 * i + s
                    max_step(b + 2, s)
                    result_step(b - 1, 1 - s)
                    norm_step(b, s)
            for b in range(B - 2, B):
                result_step(b - 1, (b - 1) % 2)
                norm_step(b, b % 2)
            result_step(B - 1, (B - 1) % 2)

        @block.tensor
        def _(pe):
            def density(g):
                for j in range(GB):
                    if j % PB == 0:
                        pe.wait_ge(x_in[(GB * g + j) // PB], 16)
                    last = pe.matmul(bank[5 * (g // 2)][QUAD * j:QUAD * (j + 1), 0:HW],
                                     dens_w[:, g % 2, :], tok[:, GB * g + j, :],
                                     start=g % 2 == 0, stop=g % 2 == 1)
                if g % 2 == 1:
                    last.then_inc(logits_done, 1)

            def fuse(i):
                if i >= 2:
                    pe.wait_ge(fused_ready, i - 1)
                pe.matmul(bank[1 + i % 2][:], fuseT[:],
                          tok[:, PB * i:PB * (i + 1), :].rearrange("p b n -> p (b n)"),
                          start=True, stop=True).then_inc(fused_done, 1)

            pe.wait_ge(dens_w_ready, 1)
            density(0)
            pe.wait_ge(par_in[1], 16)
            for t in range(2):
                last = pe.matmul(bank[7][0:E, 0:1], text_wT[:, E * t:E * (t + 1)], emb_cols[:, t:t + 1],
                                 start=t == 0, stop=t == 1)
            last.then_inc(text_done, 1)
            pe.matmul(bank[6][:, 0:C], sparse_rows, outwT, start=True, stop=True).then_inc(fuse_done, 1)
            density(1)
            pe.wait_ge(text_ready, 1)
            pe.matmul(bank[7][:, 0:1], outwT, e_sum[:], start=True, stop=True).then_inc(c_done, 1)
            pe.wait_ge(fuse_ready, 1)
            fuse(0)
            fuse(1)
            density(2)
            fuse(2)
            density(3)
            for i in range(3, NP):
                fuse(i)

            pe.wait_ge(const_ready, 1)

            def broadcast(i):
                if i >= 2:
                    pe.wait_ge(tok_ready, i - 1)
                for b in range(PB * i, PB * (i + 1)):
                    last = pe.matmul(bank[3 + i % 2][:, HW * (b % PB):HW * (b % PB + 1)],
                                     sel[:, b % HB, :], mask[:, b // HB], start=True, stop=True)
                last.then_inc(bcast_done, 1)

            def project(g):
                if g == 0:
                    pe.wait_ge(keys_ready, 2)
                if g >= 2:
                    pe.wait_ge(p0_ready, g - 1)
                for j in range(GB):
                    if j % PB == 0:
                        pe.wait_ge(tok_ready, (GB * g + j) // PB + 1)
                    last = pe.matmul(bank[5 + g % 2][QUAD * j:QUAD * (j + 1), 0:HW], wqkT,
                                     tok[:, GB * g + j, :], start=True, stop=True)
                last.then_inc(qk_done, 1)

            def values(i):
                if i == 0:
                    pe.wait_ge(c_ready, 1)
                    pe.wait_ge(wvT_ready, 1)
                if i >= 2:
                    pe.wait_ge(val_ready, i - 1)
                for c in range(PB * JC):
                    last = pe.matmul(bank[7 * (1 - i % 2)][:, 128 * c:128 * (c + 1)],
                                     tok[:, PB * i + c // JC, 128 * (c % JC):128 * (c % JC + 1)],
                                     wvT[:], start=True, stop=True)
                last.then_inc(val_done, 1)

            for h in range(2):
                pe.wait_ge(mask_ready, h + 1)
                for i in range(NP // 2 * h, NP // 2 * (h + 1)):
                    broadcast(i)
                project(2 * h)
                project(2 * h + 1)
                for i in range(NP // 2 * h, NP // 2 * (h + 1)):
                    values(i)

            def scores(b, s):
                for c in range(JC):
                    last = pe.matmul(bank[1 + s][:, HW * c:HW * (c + 1)],
                                     q_stack[:, b, 128 * c:128 * (c + 1)], k_stack[:, b, :],
                                     start=True, stop=True)
                last.then_inc(s_done, 1)

            def scores_transposed(b, s, reused):
                pe.wait_ge(shift_ready, b + 1)
                if reused:
                    pe.wait_ge(ew_ready, b - 1)
                sh = shift[:, s].rearrange("p c n -> p (c n)")
                pe.matmul(bank[3 + s][:], ones[:], sh.unsqueeze(1).to_broadcast([128, JC, HW]),
                          start=True, stop=False)
                for c in range(JC):
                    last = pe.matmul(bank[3 + s][:, HW * c:HW * (c + 1)],
                                     k_stack[:, b, 128 * c:128 * (c + 1)], q_stack[:, b, :],
                                     start=False, stop=c == JC - 1)
                last.then_inc(st_done, 1)

            def attend(b, s, reused):
                pe.wait_ge(ew_ready, b + 1)
                if reused:
                    pe.wait_ge(att_ready, b - 1)
                for c in range(JC):
                    for j in range(JC):
                        last = pe.matmul(bank[5 + s][:, HW * c:HW * c + VC],
                                         ew[:, s, j, 128 * c:128 * (c + 1)], val[:, b, j, :],
                                         start=j == 0, stop=j == JC - 1)
                last.then_inc(att_done, 1)

            def back(b, s, reused):
                pe.wait_ge(att_ready, b + 1)
                if reused:
                    pe.wait_ge(res_ready, b - 1)
                for c in range(JC):
                    last = pe.transpose(bank[7 * (1 - s)][:, 128 * c:128 * (c + 1)], att[:, s, c, :],
                                        ident[:])
                last.then_inc(back_done, 1)

            def step(b, s):
                scores_transposed(b + 1, 1 - s, True)
                scores(b + 2, s)
                back(b - 1, 1 - s, True)
                attend(b, s, True)

            pe.wait_ge(stack_in[0], 16 * 2 * NS)
            pe.wait_ge(p0_ready, G)
            pe.wait_ge(val_ready, NP)
            pe.wait_ge(ident_ready, 1)
            scores(0, 0)
            scores(1, 1)
            scores_transposed(0, 0, False)
            scores_transposed(1, 1, False)
            scores(2, 0)
            attend(0, 0, False)
            scores_transposed(2, 0, True)
            scores(3, 1)
            back(0, 0, False)
            attend(1, 1, False)
            with pe.Fori(1, HB // 2 - 1) as i:
                step(2 * i, 0)
                step(2 * i + 1, 1)
            pe.wait_ge(stack_in[1], 16 * 2 * NS)
            with pe.Fori(HB // 2 - 1, B // 2 - 1) as i:
                step(2 * i, 0)
                step(2 * i + 1, 1)
            scores_transposed(B - 1, 1, True)
            back(B - 3, 1, True)
            attend(B - 2, 0, True)
            back(B - 2, 0, True)
            attend(B - 1, 1, True)
            back(B - 1, 1, True)


_OUTS = [((16, 128, 16, 16), 'float32')]


def kernel(x, L0_conv_text_emb, L0_conv_density_w, L0_conv_density_b, L0_conv_sparse_w, L0_conv_sparse_b,
           L0_conv_text_w, L0_conv_text_b, L0_conv_out_w, L0_conv_out_b, L1_conv_Wq, L1_conv_bq, L1_conv_Wk,
           L1_conv_bk, L1_conv_Wv, L1_conv_bv, L1_conv_gamma):
    import numpy as _np
    import concourse.bacc as _bacc
    from concourse import mybir as _mybir
    from concourse.bass_utils import run_bass_kernel_spmd as _run

    C, E, T, D = x.shape[1], L0_conv_sparse_w.shape[0], L0_conv_text_w.shape[1], L1_conv_Wq.shape[0]
    columns, width = parameter_columns(C, E, T, D)
    params = _np.zeros((128, width), _np.float32)
    a = _np.asarray
    params[:, columns["density_w"]] = a(L0_conv_density_w)[:, None]
    params[:, columns["density_b"]] = a(L0_conv_density_b)
    params[:, columns["gamma"]] = a(L1_conv_gamma)[0]
    params[:, columns["bv"]] = a(L1_conv_bv)[:, None]
    params[:, columns["out_b"]] = a(L0_conv_out_b)[:, None]
    for row in range(0, 128, 2 * D):
        params[row:row + D, columns["bqk"]] = a(L1_conv_bq)[:, None]
        params[row + D:row + 2 * D, columns["bqk"]] = a(L1_conv_bk)[:, None]
    params[:, columns["wvT"]] = a(L1_conv_Wv).T
    first = columns["wqkT"].start
    params[:, first:first + D] = a(L1_conv_Wq).T
    params[:, first + D:first + 2 * D] = a(L1_conv_Wk).T
    params[0:E, columns["outwT"]] = a(L0_conv_out_w).T
    params[0:E, columns["sparse_w"]] = a(L0_conv_sparse_w)
    params[0:E, columns["sparse_b"]] = a(L0_conv_sparse_b)[:, None]
    params[0:E, columns["text_b"]] = a(L0_conv_text_b)[:, None]
    for t in range(2):
        first = columns["text_wT"].start + E * t
        params[0:T // 2, first:first + E] = a(L0_conv_text_w)[:, T // 2 * t:T // 2 * (t + 1)].T
        params[0:T // 2, columns["emb"].start + t] = a(L0_conv_text_emb)[T // 2 * t:T // 2 * (t + 1)]

    nc = _bacc.Bacc("TRN2", target_bir_lowering=False, num_devices=1)
    arrays = {"in_x_dram": _np.ascontiguousarray(x), "in_params_dram": params}
    ins = [nc.dram_tensor(name, v.shape, _mybir.dt.from_np(v.dtype), kind="ExternalInput").ap()
           for name, v in arrays.items()]
    outs = [nc.dram_tensor(f"out_{i}_dram", shape, _mybir.dt.from_np(_np.dtype(dtype)), kind="ExternalOutput").ap()
            for i, (shape, dtype) in enumerate(_OUTS)]
    sparse_fusion_attention(nc, *ins, E, T, D, *outs)
    r = _run(nc, [arrays], core_ids=[0])
    got = tuple(r.results[0][f"out_{i}_dram"] for i in range(len(_OUTS)))
    return got[0]
```

```python
from contextlib import ExitStack

import concourse.bass as bass
from concourse import mybir
from concourse.alu_op_type import AluOpType as ALU

ACT = mybir.ActivationFunctionType
AX = mybir.AxisListType
F32 = mybir.dt.float32
BF16 = mybir.dt.bfloat16
U32 = mybir.dt.uint32

TOPK = 25
SIGMOID_IS_ONE = 16.635532
SIGMOID_IS_ZERO = -88.72284
TAKEN = -3.0e38

KEY_COPIES = [3, 2, 1]


def parameter_columns(C, E, T, D):
    widths = [("density_w", 1), ("density_b", 1), ("gamma", 1), ("bv", 1), ("out_b", 1), ("bqk", 1),
              ("wvT", C), ("wqkT", 2 * D), ("outwT", C), ("sparse_w", C), ("sparse_b", 1), ("text_b", 1),
              ("text_wT", 2 * E), ("emb", 2)]
    at, columns = 0, {}
    for name, width in widths:
        columns[name] = slice(at, at + width)
        at += width
    return columns, at


def sparse_fusion_attention(nc, x, params, E, T, D, out):
    B, C, H, W = x.shape
    HW = H * W
    QUAD = 32
    GB = 128 // QUAD
    G = B // GB
    PB = 2
    NP = B // PB
    JC = HW // 128
    NS = sum(KEY_COPIES)
    KP = NS * D
    STACK_DMAS = 2 * len(KEY_COPIES)
    STACK_LOADS = [[0, 1], [2, 3]]
    HB = B // 2
    VC = C + 1
    assert C == 128 and 2 * D == QUAD and B == G * GB and KP + QUAD == 128

    COLS, PAR_COLS = parameter_columns(C, E, T, D)
    PAR_EARLY = COLS["outwT"].start

    parts_dram = nc.dram_tensor("parts_dram", (3, D, 2, B, HW), BF16, kind="Internal").ap()
    part_write = parts_dram.rearrange("t d s b n -> t b (d s) n")
    part_read = parts_dram.rearrange("t d s b n -> s (t d) (b n)")
    x_view = x.rearrange("b c h w -> c b (h w)")
    out_view = out.rearrange("b c h w -> c b (h w)")

    with ExitStack() as ctx:
        def sb(name, shape, dt=F32):
            return ctx.enter_context(nc.sbuf_tensor(name, shape, dt))

        def sem(name):
            return ctx.enter_context(nc.semaphore(name))

        bank = [ctx.enter_context(nc.psum_tensor(f"bank{i}", [128, 512], F32)) for i in range(8)]

        def block_of(name, rows):
            return par[0:rows, COLS[name]]

        tok = sb("tok", [128, B, HW])
        fused = sb("fused", [128, B, HW])
        par = sb("par", [128, PAR_COLS])
        density_w_col, density_b_col = block_of("density_w", C), block_of("density_b", 128)
        gamma_col, bv_col, out_b_col = block_of("gamma", C), block_of("bv", C), block_of("out_b", C)
        bqk_col = block_of("bqk", 128)
        wvT_raw, wqkT, outwT = block_of("wvT", C), block_of("wqkT", C), block_of("outwT", E)
        sparse_rows = block_of("sparse_w", E)
        sparse_b_col, text_b_col = block_of("sparse_b", E), block_of("text_b", E)
        text_wT, emb_cols = block_of("text_wT", T // 2), block_of("emb", T // 2)
        wvT = sb("wvT", [C, C])
        gbv = sb("gbv", [C, 1])
        fuseT = sb("fuseT", [C, C])
        e_sum = sb("e_sum", [E, 1])
        c_col = sb("c_col", [C, 1])
        table_loader = sb("table_loader", [C, 1])
        dens_w = sb("dens_w", [C, 2, QUAD])
        ident = sb("ident", [128, 128])
        idle_input = sb("idle_input", [128, 512], BF16)
        key_a = sb("key_a", [128, 2, HW])
        key_b = sb("key_b", [128, 2, HW])
        top8 = sb("top8", [128, 8])
        last8 = sb("last8", [128, 8])
        mask = sb("mask", [128, 2, HW], BF16)
        sel = sb("sel", [128, HB, 128], BF16)
        rem1 = sb("rem1", [128, 2, HW])
        parts = sb("parts", [128, G, 3, HW], BF16)
        q_stack = sb("q_stack", [128, B, HW], BF16)
        k_stack = sb("k_stack", [128, B, HW], BF16)
        val = sb("val", [128, B, JC, VC])
        neg_max = sb("neg_max", [128, 2, JC, QUAD], BF16)
        ident16 = sb("ident16", [128, 128], BF16)
        ew = sb("ew", [128, 2, JC, HW])
        rsum = sb("rsum", [128, 2, JC])
        att = sb("att", [128, 2, JC, C])

        LOGITS_BANK = [0, 7]
        MASK_BANK = [3, 4, 0, 3, 3, 4, 1, 2]
        PART_ORDER = [(0, 0), (1, 0), (0, 1), (2, 0), (1, 1), (2, 1)]
        IDLE_PRODUCTS = 8

        x_in = [sem(f"x_in{i}") for i in range(NP)]
        par_in = [sem("par_in0"), sem("par_in1")]
        idle_ready = sem("idle_ready")
        dens_w_zero = sem("dens_w_zero")
        dens_w_ready = sem("dens_w_ready")
        ident_zero = sem("ident_zero")
        ident_ready = sem("ident_ready")
        sel_zero = sem("sel_zero")
        const_ready = sem("const_ready")
        shift_const = sem("shift_const")
        wvT_ready = sem("wvT_ready")
        fuse_done = sem("fuse_done")
        fuse_ready = sem("fuse_ready")
        text_done = sem("text_done")
        text_ready = sem("text_ready")
        c_done = sem("c_done")
        c_ready = sem("c_ready")
        logits_done = sem("logits_done")
        keys_ready = sem("keys_ready")
        topk_step = sem("topk_step")
        mask_ready = sem("mask_ready")
        fused_done = sem("fused_done")
        fused_ready = sem("fused_ready")
        bcast_done = sem("bcast_done")
        tok_ready = sem("tok_ready")
        qk_done = sem("qk_done")
        qk_ready = sem("qk_ready")
        p0_ready = sem("p0_ready")
        r1_ready = sem("r1_ready")
        p1_ready = sem("p1_ready")
        p2_ready = sem("p2_ready")
        parts_out = [sem(f"parts_out{n}") for n in range(len(STACK_LOADS))]
        stack_in = [sem(f"stack_in{n}") for n in range(len(STACK_LOADS))]
        val_done = sem("val_done")
        val_ready = sem("val_ready")
        s_done = sem("s_done")
        max_ready = sem("max_ready")
        shift_done = sem("shift_done")
        shift_ready = sem("shift_ready")
        st_done = sem("st_done")
        ew_ready = sem("ew_ready")
        att_done = sem("att_done")
        rsum_ready = sem("rsum_ready")
        att_ready = sem("att_ready")
        back_done = sem("back_done")
        res_ready = sem("res_ready")
        stored = sem("stored")

        block = ctx.enter_context(nc.Block())

        @block.sync
        def _(sp):
            sp.dma_start(par[:, 0:PAR_EARLY], params[:, 0:PAR_EARLY]).then_inc(par_in[0], 16)
            for i in range(NP):
                sp.dma_start(tok[:, PB * i:PB * (i + 1), :],
                             x_view[:, PB * i:PB * (i + 1), :]).then_inc(x_in[i], 16)
                if i == 0:
                    sp.dma_start(par[:, PAR_EARLY:], params[:, PAR_EARLY:]).then_inc(par_in[1], 16)
            for n, groups in enumerate(STACK_LOADS):
                for t, k in PART_ORDER:
                    g = groups[k]
                    sp.wait_ge((p0_ready, p1_ready, p2_ready)[t], g + 1)
                    sp.dma_start(part_write[t, GB * g:GB * (g + 1)], parts[:, g, t, :]
                                 ).then_inc(parts_out[n], 16)
                sp.wait_ge(parts_out[n], 16 * 3 * len(groups))
                lo, hi = GB * groups[0], GB * (groups[-1] + 1)
                queries, keys = part_read[0, :, HW * lo:HW * hi], part_read[1, :, HW * lo:HW * hi]
                for part, copies in enumerate(KEY_COPIES):
                    first = D * sum(KEY_COPIES[:part])
                    rows = slice(first, first + D * copies)
                    sp.dma_start(q_stack[rows, lo:hi, :], queries[0:D * copies]).then_inc(stack_in[n], 16)
                    sp.dma_start(k_stack[rows, lo:hi, :],
                                 keys[D * part:D * (part + 1)].unsqueeze(0).to_broadcast(
                                     [copies, D, HW * (hi - lo)])).then_inc(stack_in[n], 16)
            def store(b):
                sp.wait_ge(res_ready, b + 1)
                sp.dma_start(out_view[:, b, :], tok[:, b, :]).then_inc(stored, 16)

            with sp.Fori(0, B - 2) as b:
                store(b)
            store(B - 2)
            store(B - 1)
            sp.wait_ge(stored, 16 * B)

        @block.gpsimd
        def _(pool):
            pool.memset(sel[:], 0.0).then_inc(sel_zero, 1)
            pool.wait_ge(sel_zero, 1)
            sel_view = sel[:].rearrange("p (g j) n -> p g j n", j=GB)
            pool.affine_select(out=sel_view, in_=sel_view, compare_op=ALU.not_equal, fill=1.0, base=0,
                               pattern=[[-1, 2], [-QUAD, GB], [0, 128]], channel_multiplier=1)
            pool.memset(val[:, :, :, C:VC], 1.0).then_inc(const_ready, 1)
            pool.memset(ident[:], 0.0).then_inc(ident_zero, 1)
            pool.wait_ge(ident_zero, 1)
            pool.affine_select(out=ident[:], in_=ident[:], compare_op=ALU.not_equal, fill=1.0, base=0,
                               pattern=[[-1, 128]], channel_multiplier=1).then_inc(ident_ready, 1)
            pool.wait_ge(ident_ready, 1)
            pool.tensor_copy(ident16[:], ident[:]).then_inc(shift_const, 1)
            pool.wait_ge(shift_const, 1)
            pool.memset(neg_max[:], 0.0).then_inc(shift_const, 1)
            pool.wait_ge(shift_const, 2)
            pool.memset(k_stack[KP:128], 1.0).then_inc(shift_const, 1)
            pool.wait_ge(shift_const, 3)
            for g in range(G):
                pool.wait_ge(p1_ready, g + 1)
                pool.tensor_tensor(parts[:, g, 2, :], rem1[:, g % 2, :], parts[:, g, 1, :], ALU.subtract
                                   ).then_inc(p2_ready, 1)

        @block.scalar
        def _(act):
            act.wait_ge(par_in[0], 16)
            act.activation(table_loader[:], gamma_col, ACT.Exp)
            act.wait_ge(c_done, 1)
            act.activation(c_col[:], bank[5][:, 0:1], ACT.Identity, bias=out_b_col).then_inc(c_ready, 1)
            act.wait_ge(c_ready, 1)

            def fused_out(i):
                act.wait_ge(fused_done, i + 1)
                act.activation(fused[:, PB * i:PB * (i + 1), :],
                               bank[1 + i % 2][:].rearrange("p (b n) -> p b n", b=PB),
                               ACT.Identity, bias=c_col[:]).then_inc(fused_ready, 1)

            def first_part(g):
                act.wait_ge(qk_done, g + 1)
                act.activation(parts[:, g, 0, :], bank[5 + g % 2][:, 0:HW], ACT.Identity, bias=bqk_col
                               ).then_inc(p0_ready, 1)

            def second_part(g):
                act.wait_ge(r1_ready, g + 1)
                act.copy(parts[:, g, 1, :], rem1[:, g % 2, :]).then_inc(p1_ready, 1)

            def val_out(i):
                act.wait_ge(val_done, i + 1)
                act.copy(val[:, PB * i:PB * (i + 1), :, 0:C],
                         bank[7 * (1 - i % 2)][:].rearrange("p (b j n) -> p b j n", b=PB, j=JC)
                         ).then_inc(val_ready, 1)

            for i in range(4):
                fused_out(i)
            first_part(0)
            fused_out(4)
            second_part(0)
            first_part(1)
            fused_out(5)
            second_part(1)
            fused_out(6)
            fused_out(7)
            act.wait_ge(const_ready, 1)
            for i in range(NP // 2):
                val_out(i)
            first_part(2)
            second_part(2)
            val_out(4)
            first_part(3)
            second_part(3)
            val_out(5)

            def exp_step(b, s, reused):
                act.wait_ge(st_done, b + 1)
                if reused:
                    act.wait_ge(att_done, b - 1)
                act.activation(ew[:, s], bank[3 + s][:].rearrange("p (j n) -> p j n", j=JC), ACT.Exp
                               ).then_inc(ew_ready, 1)

            def shift_out(b, s):
                act.wait_ge(shift_done, b + 1)
                act.copy(q_stack[KP:128, b, :], bank[1 + s][KP:128, 0:HW]).then_inc(shift_ready, 1)

            shift_out(0, 0)
            val_out(6)
            shift_out(1, 1)
            exp_step(0, 0, False)
            exp_step(1, 1, False)
            shift_out(2, 0)
            val_out(7)
            with act.Fori(1, B // 2 - 1) as i:
                for s in range(2):
                    shift_out(2 * i + s + 1, 1 - s)
                    exp_step(2 * i + s, s, True)
            shift_out(B - 1, 1)
            exp_step(B - 2, 0, True)
            exp_step(B - 1, 1, True)

        @block.vector
        def _(dve):
            steps = [0]

            def chain(ins):
                steps[0] += 1
                ins.then_inc(topk_step, 1)
                dve.wait_ge(topk_step, steps[0])

            dve.memset(idle_input[:], 0.0).then_inc(idle_ready, 1)
            dve.memset(dens_w[:], 0.0).then_inc(dens_w_zero, 1)
            dve.memset(last8[:], TAKEN)
            dve.wait_ge(dens_w_zero, 1)
            dve.wait_ge(par_in[0], 16)
            for g in range(2):
                last = dve.tensor_copy(dens_w[:, g, g:g + 1], density_w_col)
            last.then_inc(dens_w_ready, 1)
            dve.tensor_scalar(wvT[:], wvT_raw, gamma_col, None, ALU.mult)
            dve.tensor_tensor(gbv[:], bv_col, gamma_col, ALU.mult).then_inc(wvT_ready, 1)
            dve.wait_ge(par_in[1], 16)
            dve.wait_ge(fuse_done, 1)
            dve.tensor_copy(fuseT[:], bank[6][:, 0:C]).then_inc(fuse_ready, 1)
            dve.wait_ge(text_done, 1)
            dve.tensor_scalar(e_sum[:], bank[5][0:E, 0:1], sparse_b_col, text_b_col, ALU.add, ALU.add
                              ).then_inc(text_ready, 1)

            def token_step(i):
                pair = slice(PB * i, PB * (i + 1))
                dve.wait_ge(fused_ready, i + 1)
                dve.wait_ge(bcast_done, i + 1)
                dve.copy_predicated(tok[:, pair, :],
                                    bank[MASK_BANK[i]][:].rearrange("p (b n) -> p b n", b=PB).bitcast(U32),
                                    fused[:, pair, :]).then_inc(tok_ready, 1)

            def remainder(g):
                dve.wait_ge(p0_ready, g + 1)
                if g >= 2:
                    dve.wait_ge(p2_ready, g - 1)
                dve.scalar_tensor_tensor(out=rem1[:, g % 2, :], in0=bank[5 + g % 2][:, 0:HW],
                                         scalar=bqk_col, in1=parts[:, g, 0, :],
                                         op0=ALU.add, op1=ALU.subtract).then_inc(r1_ready, 1)

            def keys_out(h):
                dve.wait_ge(logits_done, h + 1)
                dve.tensor_scalar(key_b[:, h], bank[LOGITS_BANK[h]][:, 0:HW], density_b_col,
                                  SIGMOID_IS_ONE, ALU.add, ALU.min).then_inc(keys_ready, 1)

            def keys_from_below(h):
                dve.wait_ge(keys_ready, h + 1)
                chain(dve.tensor_scalar(key_a[:, h], key_b[:, h], SIGMOID_IS_ZERO, None, ALU.max))

            def top_k_round(h, r):
                keys, free = (key_a, key_b) if r % 2 == 0 else (key_b, key_a)
                chain(dve.max(top8[:], keys[:, h]))
                chain(dve.match_replace(out=free[:, h], in_to_replace=top8[:], in_values=keys[:, h],
                                        imm_value=TAKEN))

            def top_k_last(h):
                chain(dve.max(top8[:], key_b[:, h]))
                chain(dve.tensor_copy(last8[:, 0:TOPK % 8], top8[:, 0:TOPK % 8]))
                chain(dve.match_replace(out=key_a[:, h], in_to_replace=last8[:], in_values=key_b[:, h],
                                        imm_value=TAKEN))
                dve.tensor_scalar(mask[:, h], key_a[:, h], TAKEN, None, ALU.is_equal
                                  ).then_inc(mask_ready, 1)

            assert TOPK // 8 == 3
            keys_out(0)
            keys_from_below(0)
            for r in range(3):
                top_k_round(0, r)
            top_k_last(0)
            keys_out(1)
            for i in range(NP // 2):
                token_step(i)
            remainder(0)
            keys_from_below(1)
            top_k_round(1, 0)
            remainder(1)
            top_k_round(1, 1)
            top_k_round(1, 2)
            top_k_last(1)
            for i in range(NP // 2, NP):
                token_step(i)
            remainder(2)
            remainder(3)

            def max_step(b, s):
                dve.wait_ge(s_done, b + 1)
                dve.tensor_reduce(neg_max[:, s, :, 0], bank[1 + s][:].rearrange("p (c n) -> p c n", c=JC),
                                  axis=AX.X, op=ALU.max, negate=True).then_inc(max_ready, 1)

            def norm_step(b, s):
                o = bank[5 + s][:].rearrange("p (c n) -> p c n", c=JC)
                dve.wait_ge(att_done, b + 1)
                dve.reciprocal(rsum[:, s, :], o[:, :, C]).then_inc(rsum_ready, 1)
                dve.wait_ge(rsum_ready, b + 1)
                dve.tensor_tensor(att[:, s], o[:, :, 0:C],
                                  rsum[:, s, :].unsqueeze(2).to_broadcast([128, JC, C]),
                                  ALU.mult).then_inc(att_ready, 1)

            def result_step(b, s):
                dve.wait_ge(back_done, b + 1)
                dve.scalar_tensor_tensor(out=tok[:, b, :], in0=bank[7 * (1 - s)][:, 0:HW],
                                         scalar=gbv[:], in1=tok[:, b, :],
                                         op0=ALU.add, op1=ALU.add).then_inc(res_ready, 1)

            dve.wait_ge(wvT_ready, 1)
            dve.wait_ge(shift_const, 3)
            for b in range(4):
                max_step(b, b % 2)
            norm_step(0, 0)
            max_step(4, 0)
            norm_step(1, 1)
            result_step(0, 0)
            with dve.Fori(1, B // 2 - 2) as i:
                for s in range(2):
                    max_step(2 * i + s + 3, 1 - s)
                    norm_step(2 * i + s, s)
                    result_step(2 * i + s - 1, 1 - s)
            for b in range(B - 4, B):
                if b + 3 < B:
                    max_step(b + 3, (b + 3) % 2)
                norm_step(b, b % 2)
                result_step(b - 1, (b - 1) % 2)
            result_step(B - 1, (B - 1) % 2)

        @block.tensor
        def _(pe):
            def density(g):
                for j in range(GB):
                    if j % PB == 0:
                        pe.wait_ge(x_in[(GB * g + j) // PB], 16)
                    last = pe.matmul(bank[LOGITS_BANK[g // 2]][QUAD * j:QUAD * (j + 1), 0:HW],
                                     dens_w[:, g % 2, :], tok[:, GB * g + j, :],
                                     start=g % 2 == 0, stop=g % 2 == 1)
                if g % 2 == 1:
                    last.then_inc(logits_done, 1)

            def fuse(i):
                if i >= 2:
                    pe.wait_ge(fused_ready, i - 1)
                pe.matmul(bank[1 + i % 2][:], fuseT[:],
                          tok[:, PB * i:PB * (i + 1), :].rearrange("p b n -> p (b n)"),
                          start=True, stop=True).then_inc(fused_done, 1)

            pe.wait_ge(idle_ready, 1)
            for _ in range(IDLE_PRODUCTS):
                pe.matmul(bank[3][:], idle_input[:, 0:128], idle_input[:], start=True, stop=True)
            pe.wait_ge(dens_w_ready, 1)
            density(0)
            pe.wait_ge(par_in[1], 16)
            pe.matmul(bank[6][:, 0:C], sparse_rows, outwT, start=True, stop=True).then_inc(fuse_done, 1)
            density(1)
            for t in range(2):
                last = pe.matmul(bank[5][0:E, 0:1], text_wT[:, E * t:E * (t + 1)], emb_cols[:, t:t + 1],
                                 start=t == 0, stop=t == 1)
            last.then_inc(text_done, 1)
            pe.wait_ge(fuse_ready, 1)
            fuse(0)
            pe.wait_ge(text_ready, 1)
            pe.matmul(bank[5][:, 0:1], outwT, e_sum[:], start=True, stop=True).then_inc(c_done, 1)
            fuse(1)
            density(2)
            density(3)
            fuse(2)
            fuse(3)

            def broadcast(i):
                if i == 2:
                    pe.wait_ge(keys_ready, 1)
                if i == 3:
                    pe.wait_ge(tok_ready, 1)
                if i == 4:
                    pe.wait_ge(tok_ready, 4)
                if i == 6:
                    pe.wait_ge(fused_ready, NP)
                for b in range(PB * i, PB * (i + 1)):
                    last = pe.matmul(bank[MASK_BANK[i]][:, HW * (b % PB):HW * (b % PB + 1)],
                                     sel[:, b % HB, :], mask[:, b // HB], start=True, stop=True)
                last.then_inc(bcast_done, 1)

            def project(g):
                if g == 0:
                    pe.wait_ge(c_ready, 1)
                if g >= 2:
                    pe.wait_ge(r1_ready, g - 1)
                for j in range(GB):
                    if j % PB == 0:
                        pe.wait_ge(tok_ready, (GB * g + j) // PB + 1)
                    last = pe.matmul(bank[5 + g % 2][QUAD * j:QUAD * (j + 1), 0:HW], wqkT,
                                     tok[:, GB * g + j, :], start=True, stop=True)
                last.then_inc(qk_done, 1)

            def values(i):
                if i == 0:
                    pe.wait_ge(keys_ready, 2)
                    pe.wait_ge(wvT_ready, 1)
                if i >= 2:
                    pe.wait_ge(val_ready, i - 1)
                for c in range(PB * JC):
                    last = pe.matmul(bank[7 * (1 - i % 2)][:, 128 * c:128 * (c + 1)],
                                     tok[:, PB * i + c // JC, 128 * (c % JC):128 * (c % JC + 1)],
                                     wvT[:], start=True, stop=True)
                last.then_inc(val_done, 1)

            pe.wait_ge(const_ready, 1)
            pe.wait_ge(mask_ready, 1)
            broadcast(0)
            broadcast(1)
            broadcast(2)
            fuse(4)
            project(0)
            broadcast(3)
            project(1)
            fuse(5)
            fuse(6)
            fuse(7)
            values(0)
            values(1)
            values(2)
            pe.wait_ge(mask_ready, 2)
            for i in range(NP // 2, NP):
                broadcast(i)
            values(3)
            project(2)
            values(4)
            project(3)
            values(5)

            def scores(b, s):
                for c in range(JC):
                    last = pe.matmul(bank[1 + s][:, HW * c:HW * (c + 1)],
                                     q_stack[0:KP, b, 128 * c:128 * (c + 1)], k_stack[0:KP, b, :],
                                     start=True, stop=True)
                last.then_inc(s_done, 1)

            def shift(b, s):
                pe.wait_ge(max_ready, b + 1)
                for c in range(JC):
                    last = pe.matmul(bank[1 + s][KP:128, 128 * c:128 * (c + 1)], neg_max[:, s, c, :],
                                     ident16[:], start=True, stop=True)
                last.then_inc(shift_done, 1)

            def scores_transposed(b, s, reused):
                pe.wait_ge(shift_ready, b + 1)
                if reused:
                    pe.wait_ge(ew_ready, b - 1)
                for c in range(JC):
                    last = pe.matmul(bank[3 + s][:, HW * c:HW * (c + 1)],
                                     k_stack[:, b, 128 * c:128 * (c + 1)], q_stack[:, b, :],
                                     start=True, stop=True)
                last.then_inc(st_done, 1)

            def attend(b, s, reused):
                pe.wait_ge(ew_ready, b + 1)
                if reused:
                    pe.wait_ge(att_ready, b - 1)
                for c in range(JC):
                    for j in range(JC):
                        last = pe.matmul(bank[5 + s][:, HW * c:HW * c + VC],
                                         ew[:, s, j, 128 * c:128 * (c + 1)], val[:, b, j, :],
                                         start=j == 0, stop=j == JC - 1)
                last.then_inc(att_done, 1)

            def back(b, s, reused):
                pe.wait_ge(att_ready, b + 1)
                if reused:
                    pe.wait_ge(res_ready, b - 1)
                for c in range(JC):
                    last = pe.transpose(bank[7 * (1 - s)][:, 128 * c:128 * (c + 1)], att[:, s, c, :],
                                        ident[:])
                last.then_inc(back_done, 1)

            def step(b, s):
                scores_transposed(b + 1, 1 - s, True)
                scores(b + 3, 1 - s)
                shift(b + 2, s)
                attend(b, s, True)
                back(b - 1, 1 - s, True)

            pe.wait_ge(stack_in[0], 16 * STACK_DMAS)
            pe.wait_ge(tok_ready, NP)
            pe.wait_ge(shift_const, 3)
            scores(0, 0)
            scores(1, 1)
            values(6)
            shift(0, 0)
            values(7)
            shift(1, 1)
            pe.wait_ge(shift_ready, 1)
            scores(2, 0)
            scores_transposed(0, 0, False)
            scores_transposed(1, 1, False)
            scores(3, 1)
            shift(2, 0)
            pe.wait_ge(r1_ready, G)
            pe.wait_ge(val_ready, NP - 2)
            attend(0, 0, False)
            scores_transposed(2, 0, True)
            scores(4, 0)
            shift(3, 1)
            attend(1, 1, False)
            pe.wait_ge(val_ready, NP)
            pe.wait_ge(ident_ready, 1)
            back(0, 0, False)
            with pe.Fori(1, HB // 2 - 2) as i:
                step(2 * i, 0)
                step(2 * i + 1, 1)
            step(HB - 4, 0)
            pe.wait_ge(stack_in[1], 16 * STACK_DMAS)
            step(HB - 3, 1)
            with pe.Fori(HB // 2 - 1, B // 2 - 2) as i:
                step(2 * i, 0)
                step(2 * i + 1, 1)
            step(B - 4, 0)
            for b in range(B - 3, B):
                if b + 1 < B:
                    scores_transposed(b + 1, (b + 1) % 2, True)
                if b + 2 < B:
                    shift(b + 2, b % 2)
                attend(b, b % 2, True)
                back(b - 1, (b - 1) % 2, True)
            back(B - 1, 1, True)


_OUTS = [((16, 128, 16, 16), 'float32')]


def kernel(x, L0_conv_text_emb, L0_conv_density_w, L0_conv_density_b, L0_conv_sparse_w, L0_conv_sparse_b,
           L0_conv_text_w, L0_conv_text_b, L0_conv_out_w, L0_conv_out_b, L1_conv_Wq, L1_conv_bq, L1_conv_Wk,
           L1_conv_bk, L1_conv_Wv, L1_conv_bv, L1_conv_gamma):
    import numpy as _np
    import concourse.bacc as _bacc
    from concourse import mybir as _mybir
    from concourse.bass_utils import run_bass_kernel_spmd as _run

    C, E, T, D = x.shape[1], L0_conv_sparse_w.shape[0], L0_conv_text_w.shape[1], L1_conv_Wq.shape[0]
    columns, width = parameter_columns(C, E, T, D)
    params = _np.zeros((128, width), _np.float32)
    a = _np.asarray
    params[:, columns["density_w"]] = a(L0_conv_density_w)[:, None]
    params[:, columns["density_b"]] = a(L0_conv_density_b)
    params[:, columns["gamma"]] = a(L1_conv_gamma)[0]
    params[:, columns["bv"]] = a(L1_conv_bv)[:, None]
    params[:, columns["out_b"]] = a(L0_conv_out_b)[:, None]
    for row in range(0, 128, 2 * D):
        params[row:row + 2 * D:2, columns["bqk"]] = a(L1_conv_bq)[:, None]
        params[row + 1:row + 2 * D:2, columns["bqk"]] = a(L1_conv_bk)[:, None]
    params[:, columns["wvT"]] = a(L1_conv_Wv).T
    first = columns["wqkT"].start
    params[:, first:first + 2 * D:2] = a(L1_conv_Wq).T
    params[:, first + 1:first + 2 * D:2] = a(L1_conv_Wk).T
    params[0:E, columns["outwT"]] = a(L0_conv_out_w).T
    params[0:E, columns["sparse_w"]] = a(L0_conv_sparse_w)
    params[0:E, columns["sparse_b"]] = a(L0_conv_sparse_b)[:, None]
    params[0:E, columns["text_b"]] = a(L0_conv_text_b)[:, None]
    for t in range(2):
        first = columns["text_wT"].start + E * t
        params[0:T // 2, first:first + E] = a(L0_conv_text_w)[:, T // 2 * t:T // 2 * (t + 1)].T
        params[0:T // 2, columns["emb"].start + t] = a(L0_conv_text_emb)[T // 2 * t:T // 2 * (t + 1)]

    nc = _bacc.Bacc("TRN2", target_bir_lowering=False, num_devices=1)
    arrays = {"in_x_dram": _np.ascontiguousarray(x), "in_params_dram": params}
    ins = [nc.dram_tensor(name, v.shape, _mybir.dt.from_np(v.dtype), kind="ExternalInput").ap()
           for name, v in arrays.items()]
    outs = [nc.dram_tensor(f"out_{i}_dram", shape, _mybir.dt.from_np(_np.dtype(dtype)), kind="ExternalOutput").ap()
            for i, (shape, dtype) in enumerate(_OUTS)]
    sparse_fusion_attention(nc, *ins, E, T, D, *outs)
    r = _run(nc, [arrays], core_ids=[0])
    got = tuple(r.results[0][f"out_{i}_dram"] for i in range(len(_OUTS)))
    return got[0]
```
